# Optimizing a Trainium2 kernel written in Bass

```python
import numpy as np
import jax
import jax.numpy as jnp

def _softmax(x, axis=-1):
    return jax.nn.softmax(x, axis=axis)

def _gelu(x):
    return jax.nn.gelu(x, approximate=True)

def _silu(x):
    return jax.nn.silu(x)

def _sigmoid(x):
    return jax.nn.sigmoid(x)

def _layernorm(x, axis=-1, eps=1e-05):
    m = jnp.mean(x, axis=axis, keepdims=True)
    v = jnp.var(x, axis=axis, keepdims=True)
    return (x - m) / jnp.sqrt(v + eps)

def _scatter_add(tgt, idx, src, axis=0):
    return tgt.at[idx].add(src)

def _segment_sum(src, seg, n):
    return jax.ops.segment_sum(src, seg, n)
kernel_name = 'mk_dlrm_tower_d1_rec_r8_4d5736'

def setup_inputs(seed: int=0):
    np.random.seed(seed)
    _w = jnp.asarray

    def _rec_inputs():
        import jax
        import jax.numpy as jnp
        _tk = jax.random.key(seed)
        dense_ctx = jax.random.normal(jax.random.fold_in(_tk, 190), (512, 16), jnp.float32)
        ids = jnp.stack([jax.random.randint(jax.random.fold_in(_tk, 200 + f), (512,), 0, v, jnp.int32) for f, v in enumerate([1250, 1000, 1000, 1250, 1250, 1000, 1000, 12500, 1000, 1000, 1250, 12500, 1000, 1000, 1250, 1000, 1250, 1250, 12500, 1000, 1000, 1250, 1250, 1000, 1000, 1000, 12500, 1000, 12500, 1250, 12500, 1250])], axis=1)
        tbl_0 = 0.05 * jax.random.normal(jax.random.fold_in(_tk, 500 + 0), (1250, 256), jnp.float32)
        tbl_1 = 0.05 * jax.random.normal(jax.random.fold_in(_tk, 500 + 1), (1000, 256), jnp.float32)
        tbl_2 = 0.05 * jax.random.normal(jax.random.fold_in(_tk, 500 + 2), (1000, 256), jnp.float32)
        tbl_3 = 0.05 * jax.random.normal(jax.random.fold_in(_tk, 500 + 3), (1250, 256), jnp.float32)
        tbl_4 = 0.05 * jax.random.normal(jax.random.fold_in(_tk, 500 + 4), (1250, 256), jnp.float32)
        tbl_5 = 0.05 * jax.random.normal(jax.random.fold_in(_tk, 500 + 5), (1000, 256), jnp.float32)
        tbl_6 = 0.05 * jax.random.normal(jax.random.fold_in(_tk, 500 + 6), (1000, 256), jnp.float32)
        tbl_7 = 0.05 * jax.random.normal(jax.random.fold_in(_tk, 500 + 7), (12500, 256), jnp.float32)
        tbl_8 = 0.05 * jax.random.normal(jax.random.fold_in(_tk, 500 + 8), (1000, 256), jnp.float32)
        tbl_9 = 0.05 * jax.random.normal(jax.random.fold_in(_tk, 500 + 9), (1000, 256), jnp.float32)
        tbl_10 = 0.05 * jax.random.normal(jax.random.fold_in(_tk, 500 + 10), (1250, 256), jnp.float32)
        tbl_11 = 0.05 * jax.random.normal(jax.random.fold_in(_tk, 500 + 11), (12500, 256), jnp.float32)
        tbl_12 = 0.05 * jax.random.normal(jax.random.fold_in(_tk, 500 + 12), (1000, 256), jnp.float32)
        tbl_13 = 0.05 * jax.random.normal(jax.random.fold_in(_tk, 500 + 13), (1000, 256), jnp.float32)
        tbl_14 = 0.05 * jax.random.normal(jax.random.fold_in(_tk, 500 + 14), (1250, 256), jnp.float32)
        tbl_15 = 0.05 * jax.random.normal(jax.random.fold_in(_tk, 500 + 15), (1000, 256), jnp.float32)
        tbl_16 = 0.05 * jax.random.normal(jax.random.fold_in(_tk, 500 + 16), (1250, 256), jnp.float32)
        tbl_17 = 0.05 * jax.random.normal(jax.random.fold_in(_tk, 500 + 17), (1250, 256), jnp.float32)
        tbl_18 = 0.05 * jax.random.normal(jax.random.fold_in(_tk, 500 + 18), (12500, 256), jnp.float32)
        tbl_19 = 0.05 * jax.random.normal(jax.random.fold_in(_tk, 500 + 19), (1000, 256), jnp.float32)
        tbl_20 = 0.05 * jax.random.normal(jax.random.fold_in(_tk, 500 + 20), (1000, 256), jnp.float32)
        tbl_21 = 0.05 * jax.random.normal(jax.random.fold_in(_tk, 500 + 21), (1250, 256), jnp.float32)
        tbl_22 = 0.05 * jax.random.normal(jax.random.fold_in(_tk, 500 + 22), (1250, 256), jnp.float32)
        tbl_23 = 0.05 * jax.random.normal(jax.random.fold_in(_tk, 500 + 23), (1000, 256), jnp.float32)
        tbl_24 = 0.05 * jax.random.normal(jax.random.fold_in(_tk, 500 + 24), (1000, 256), jnp.float32)
        tbl_25 = 0.05 * jax.random.normal(jax.random.fold_in(_tk, 500 + 25), (1000, 256), jnp.float32)
        tbl_26 = 0.05 * jax.random.normal(jax.random.fold_in(_tk, 500 + 26), (12500, 256), jnp.float32)
        tbl_27 = 0.05 * jax.random.normal(jax.random.fold_in(_tk, 500 + 27), (1000, 256), jnp.float32)
        tbl_28 = 0.05 * jax.random.normal(jax.random.fold_in(_tk, 500 + 28), (12500, 256), jnp.float32)
        tbl_29 = 0.05 * jax.random.normal(jax.random.fold_in(_tk, 500 + 29), (1250, 256), jnp.float32)
        tbl_30 = 0.05 * jax.random.normal(jax.random.fold_in(_tk, 500 + 30), (12500, 256), jnp.float32)
        tbl_31 = 0.05 * jax.random.normal(jax.random.fold_in(_tk, 500 + 31), (1250, 256), jnp.float32)
        _rk = jax.random.fold_in(_tk, 7)
        W_top1 = 0.0441942 * jax.random.normal(jax.random.fold_in(_tk, 801), (512, 512), jnp.float32)
        W_top2 = 0.0441942 * jax.random.normal(jax.random.fold_in(_tk, 802), (512, 256), jnp.float32)
        W_top3 = 0.0625 * jax.random.normal(jax.random.fold_in(_tk, 803), (256, 1), jnp.float32)
        b_top1 = jnp.zeros((512,), jnp.float32)
        b_top2 = jnp.zeros((256,), jnp.float32)
        return (dense_ctx, ids, tbl_0, tbl_1, tbl_2, tbl_3, tbl_4, tbl_5, tbl_6, tbl_7, tbl_8, tbl_9, tbl_10, tbl_11, tbl_12, tbl_13, tbl_14, tbl_15, tbl_16, tbl_17, tbl_18, tbl_19, tbl_20, tbl_21, tbl_22, tbl_23, tbl_24, tbl_25, tbl_26, tbl_27, tbl_28, tbl_29, tbl_30, tbl_31, W_top1, b_top1, W_top2, b_top2, W_top3)
    dense_ctx, ids, tbl_0, tbl_1, tbl_2, tbl_3, tbl_4, tbl_5, tbl_6, tbl_7, tbl_8, tbl_9, tbl_10, tbl_11, tbl_12, tbl_13, tbl_14, tbl_15, tbl_16, tbl_17, tbl_18, tbl_19, tbl_20, tbl_21, tbl_22, tbl_23, tbl_24, tbl_25, tbl_26, tbl_27, tbl_28, tbl_29, tbl_30, tbl_31, W_top1, b_top1, W_top2, b_top2, W_top3 = _rec_inputs()

    def _L0_rec_setup():
        import jax, jax.numpy as jnp
        import numpy as np
        B, N, D = (1024, 32, 256)
        key = jax.random.key(seed)
        x = jax.random.normal(key, (B, N, D), dtype=jnp.float32)
        return {'x': x}
    _L0_rec_all = _L0_rec_setup()
    _L0_rec_in = {k: v for k, v in _L0_rec_all.items() if k in ()}
    del _L0_rec_all
    return {'dense_ctx': dense_ctx, 'ids': ids, 'tbl_0': tbl_0, 'tbl_1': tbl_1, 'tbl_2': tbl_2, 'tbl_3': tbl_3, 'tbl_4': tbl_4, 'tbl_5': tbl_5, 'tbl_6': tbl_6, 'tbl_7': tbl_7, 'tbl_8': tbl_8, 'tbl_9': tbl_9, 'tbl_10': tbl_10, 'tbl_11': tbl_11, 'tbl_12': tbl_12, 'tbl_13': tbl_13, 'tbl_14': tbl_14, 'tbl_15': tbl_15, 'tbl_16': tbl_16, 'tbl_17': tbl_17, 'tbl_18': tbl_18, 'tbl_19': tbl_19, 'tbl_20': tbl_20, 'tbl_21': tbl_21, 'tbl_22': tbl_22, 'tbl_23': tbl_23, 'tbl_24': tbl_24, 'tbl_25': tbl_25, 'tbl_26': tbl_26, 'tbl_27': tbl_27, 'tbl_28': tbl_28, 'tbl_29': tbl_29, 'tbl_30': tbl_30, 'tbl_31': tbl_31, 'W_top1': W_top1, 'b_top1': b_top1, 'W_top2': W_top2, 'b_top2': b_top2, 'W_top3': W_top3}

def reference(dense_ctx, ids, tbl_0, tbl_1, tbl_2, tbl_3, tbl_4, tbl_5, tbl_6, tbl_7, tbl_8, tbl_9, tbl_10, tbl_11, tbl_12, tbl_13, tbl_14, tbl_15, tbl_16, tbl_17, tbl_18, tbl_19, tbl_20, tbl_21, tbl_22, tbl_23, tbl_24, tbl_25, tbl_26, tbl_27, tbl_28, tbl_29, tbl_30, tbl_31, W_top1, b_top1, W_top2, b_top2, W_top3):
    import jax
    import jax.numpy as jnp

    def _L0_rec_ref(x):
        import jax, jax.numpy as jnp
        import numpy as np
        B, N, D = (1024, 32, 256)
        'Second-order feature interaction (DLRM dot interaction).\n\n            Computes dot(x_i, x_j) for all field pairs i < j (self_interaction=False),\n            flattened in row-major upper-triangular order -> [B, N*(N-1)/2].\n            Matches tf.boolean_mask(dot_products, strictly_upper_mask) ordering.\n            '
        b, n, d = x.shape
        iu, ju = jnp.triu_indices(n, k=1)
        dots = jnp.einsum('bnd,bmd->bnm', x, x)
        return dots[:, iu, ju]
    e = jnp.stack([tbl_0[ids[:, 0]], tbl_1[ids[:, 1]], tbl_2[ids[:, 2]], tbl_3[ids[:, 3]], tbl_4[ids[:, 4]], tbl_5[ids[:, 5]], tbl_6[ids[:, 6]], tbl_7[ids[:, 7]], tbl_8[ids[:, 8]], tbl_9[ids[:, 9]], tbl_10[ids[:, 10]], tbl_11[ids[:, 11]], tbl_12[ids[:, 12]], tbl_13[ids[:, 13]], tbl_14[ids[:, 14]], tbl_15[ids[:, 15]], tbl_16[ids[:, 16]], tbl_17[ids[:, 17]], tbl_18[ids[:, 18]], tbl_19[ids[:, 19]], tbl_20[ids[:, 20]], tbl_21[ids[:, 21]], tbl_22[ids[:, 22]], tbl_23[ids[:, 23]], tbl_24[ids[:, 24]], tbl_25[ids[:, 25]], tbl_26[ids[:, 26]], tbl_27[ids[:, 27]], tbl_28[ids[:, 28]], tbl_29[ids[:, 29]], tbl_30[ids[:, 30]], tbl_31[ids[:, 31]]], axis=1)
    z = _L0_rec_ref(e)
    z = z.reshape(z.shape[0], -1)
    h = jnp.concatenate([z, dense_ctx], axis=1)
    h = jnp.maximum(h @ W_top1 + b_top1, 0.0)
    h = jnp.maximum(h @ W_top2 + b_top2, 0.0)
    y = h @ W_top3
    return y

_drawn_inputs = setup_inputs


def setup_inputs(seed=0):
    import zlib

    import numpy as np

    out = dict(_drawn_inputs(seed))
    spreads = {'b_top1': (0.0, 0.1), 'b_top2': (0.0, 0.1)}
    factors = {}
    for name, (base, spread) in spreads.items():
        noise = np.random.default_rng([zlib.crc32(name.encode()), seed]).standard_normal(out[name].shape)
        drawn = base * np.exp(spread * noise) if base else spread * noise
        out[name] = jnp.asarray(drawn.astype(out[name].dtype))
    for name, factor in factors.items():
        out[name] = (out[name] * factor).astype(out[name].dtype)
    return out
```

```python
from contextlib import ExitStack

import concourse.bass as bass
from concourse import mybir

P = 128
F = 32
D = 256
B = 512
DENSE = 16
H1, H2 = 512, 256
KD = D // P
EX = P // F
TILE = 128
TILES = B // TILE
SLOTS = TILE // EX
PAIRS = SLOTS // 2
BLOCKS = 4
BP = PAIRS // BLOCKS
BG = SLOTS // BLOCKS
BE = TILE // BLOCKS
QJ = F // EX
N1, N2 = H1 // P, H2 // P


def dlrm_program(nc, tables, row_ids, row_base, dense_t, identity, w1, b1, w2, b2, w3, y):
    f32, i32 = mybir.dt.float32, mybir.dt.int32
    ACT = mybir.ActivationFunctionType
    ALU = mybir.AluOpType

    with ExitStack() as ctx:
        def sb(name, shape, dt=f32):
            return ctx.enter_context(nc.sbuf_tensor(name, shape, dt))

        def ps(name, shape):
            return ctx.enter_context(nc.psum_tensor(name, shape, f32))

        def sem(name):
            return ctx.enter_context(nc.semaphore(name))

        ids_sb = sb("ids_sb", [P, B // EX], i32)
        base_sb = sb("base_sb", [P, B // EX], i32)
        row_idx = sb("row_idx", [P, B // EX], i32)
        tile_idx = sb("tile_idx", [P, SLOTS], i32)
        ident = sb("ident", [P, P])
        emb = sb("emb", [P, SLOTS, D])
        emb_t = sb("emb_t", [P, 2, 2, KD, P])
        feat = sb("feat", [P, QJ, TILE])
        dense_sb = sb("dense_sb", [DENSE, B])
        w1_sb = sb("w1_sb", [P, QJ, H1])
        w2_sb = sb("w2_sb", [P, N1, H2])
        w3_sb = sb("w3_sb", [P, N2])
        b1_sb = sb("b1_sb", [P, N1])
        b2_sb = sb("b2_sb", [P, N2])
        h1 = sb("h1", [P, N1, TILE])
        h2 = sb("h2", [P, N2, TILE])
        y_sb = sb("y_sb", [1, B])

        tr_ps = [ps(f"tr_ps{i}", [P, 2, KD, P]) for i in range(2)]
        dots_ps = [ps(f"dots_ps{i}", [P, BG, P]) for i in range(2)]
        h1_ps = ps("h1_ps", [P, N1, TILE])
        out_ps = ps("out_ps", [P, 4, TILE])

        ids_loaded = sem("ids_loaded")
        ident_loaded = sem("ident_loaded")
        dense_loaded = sem("dense_loaded")
        weights_loaded = sem("weights_loaded")
        idx_based = sem("idx_based")
        idx_ready = sem("idx_ready")
        gathered = [sem(f"gathered{p}") for p in range(PAIRS)]
        blocks_begun = sem("blocks_begun")
        transposed = sem("transposed")
        emb_t_ready = sem("emb_t_ready")
        dots_done = sem("dots_done")
        extracted = sem("extracted")
        feat_cleared = sem("feat_cleared")
        l1_done = sem("l1_done")
        h1_ready = sem("h1_ready")
        l2_done = sem("l2_done")
        h2_ready = sem("h2_ready")
        l3_done = sem("l3_done")
        y_ready = sem("y_ready")
        y_stored = sem("y_stored")

        block = ctx.enter_context(nc.Block())

        @block.sync
        def _(sp):
            sp.dma_start(ids_sb[:], row_ids).then_inc(ids_loaded, 16)
            sp.dma_start(base_sb[:], row_base).then_inc(ids_loaded, 16)
            sp.dma_start(ident[:], identity).then_inc(ident_loaded, 16)
            sp.dma_start(dense_sb[:], dense_t).then_inc(dense_loaded, 16)
            sp.dma_start(w1_sb[:], w1).then_inc(weights_loaded, 16)
            sp.dma_start(w2_sb[:], w2).then_inc(weights_loaded, 16)
            sp.dma_start(w3_sb[:], w3).then_inc(weights_loaded, 16)
            sp.dma_start(b1_sb[:], b1).then_inc(weights_loaded, 16)
            sp.dma_start(b2_sb[:], b2).then_inc(weights_loaded, 16)
            sp.wait_ge(y_ready, TILES)
            sp.dma_start(y, y_sb[:]).then_inc(y_stored, 16)
            sp.wait_ge(y_stored, 16)

        @block.gpsimd
        def _(pool):
            def gather_tile(t, ring_used):
                for slot in range(SLOTS):
                    if slot % BG == 0:
                        b = slot // BG
                        pool.wait_ge(idx_ready, t * BLOCKS + b + 1)
                        if ring_used:
                            pool.wait_ge(transposed, (t - 1) * PAIRS + (b + 1) * BP)
                        pool.sem_inc(blocks_begun, 1)
                    nc.gpsimd.indirect_dma_start(
                        emb[:, slot, :], None, tables,
                        bass.IndirectOffsetOnAxis(tile_idx[:, slot:slot + 1], 0),
                    ).then_inc(gathered[slot // 2], 16)

            gather_tile(0, False)
            with pool.Fori(1, TILES) as t:
                gather_tile(t, True)

        @block.tensor
        def _(pe):
            def transpose_pair(t, p):
                pe.wait_ge(gathered[p], 32 * t + 32)
                for s in range(2):
                    for c in range(KD):
                        last = nc.tensor.transpose(tr_ps[p % 2][:, s, c, :],
                                                   emb[:, 2 * p + s, c * P:(c + 1) * P], ident[:])
                last.then_inc(transposed, 1)

            def dots_of_pair(t, p, buffer_used):
                b = p // BP
                pe.wait_ge(emb_t_ready, t * PAIRS + p + 1)
                if p % BP == 0 and buffer_used:
                    pe.wait_ge(extracted, t * BLOCKS + b - 1)
                for s in range(2):
                    for c in range(KD):
                        operand = emb_t[:, p % 2, s, c, :]
                        last = nc.tensor.matmul(dots_ps[b % 2][:, 2 * (p % BP) + s, :], operand, operand,
                                                start=(c == 0), stop=(c == KD - 1))
                if p % BP == BP - 1:
                    last.then_inc(dots_done, 1)

            def interact(t, blocks, buffer_used):
                pairs = [b * BP + k for b in blocks for k in range(BP)]
                transpose_pair(t, pairs[0])
                for p in pairs:
                    if p != pairs[-1]:
                        transpose_pair(t, p + 1)
                    dots_of_pair(t, p, buffer_used or p // BP >= 2)

            def top_network(t):
                pe.wait_ge(extracted, t * BLOCKS + BLOCKS)
                for n in range(N1):
                    for j in range(QJ):
                        last = nc.tensor.matmul(h1_ps[:, n, :], w1_sb[:, j, n * P:(n + 1) * P], feat[:, j, :],
                                                start=(j == 0), stop=(j == QJ - 1))
                last.then_inc(l1_done, 1)
                pe.wait_ge(h1_ready, t + 1)
                for n in range(N2):
                    for k in range(N1):
                        last = nc.tensor.matmul(out_ps[:, n, :], w2_sb[:, k, n * P:(n + 1) * P], h1[:, k, :],
                                                start=(k == 0), stop=(k == N1 - 1))
                last.then_inc(l2_done, 1)
                pe.wait_ge(h2_ready, t + 1)
                for k in range(N2):
                    last = nc.tensor.matmul(out_ps[0:1, N2, :], w3_sb[:, k:k + 1], h2[:, k, :],
                                            start=(k == 0), stop=(k == N2 - 1))
                last.then_inc(l3_done, 1)

            pe.wait_ge(ident_loaded, 16)
            interact(0, range(BLOCKS), False)
            pe.wait_ge(weights_loaded, 5 * 16)
            with pe.Fori(1, TILES) as t:
                interact(t, [0], True)
                top_network(t - 1)
                interact(t, range(1, BLOCKS), True)
            top_network(TILES - 1)

        @block.scalar
        def _(act):
            def copy_transposed(t, blocks):
                for b in blocks:
                    for p in range(b * BP, (b + 1) * BP):
                        act.wait_ge(transposed, t * PAIRS + p + 1)
                        nc.scalar.copy(emb_t[:, p % 2, :, :, :], tr_ps[p % 2][:, :, :, :]).then_inc(emb_t_ready, 1)

            def top_network(t):
                act.wait_ge(l1_done, t + 1)
                for n in range(N1):
                    last = nc.scalar.activation(h1[:, n, :], h1_ps[:, n, :], ACT.Relu, bias=b1_sb[:, n:n + 1])
                last.then_inc(h1_ready, 1)
                act.wait_ge(l2_done, t + 1)
                for n in range(N2):
                    last = nc.scalar.activation(h2[:, n, :], out_ps[:, n, :], ACT.Relu, bias=b2_sb[:, n:n + 1])
                last.then_inc(h2_ready, 1)
                act.wait_ge(l3_done, t + 1)
                nc.scalar.copy(y_sb[:, bass.ds(t * TILE, TILE)], out_ps[0:1, N2, :]).then_inc(y_ready, 1)

            copy_transposed(0, range(BLOCKS))
            act.wait_ge(weights_loaded, 5 * 16)
            with act.Fori(1, TILES) as t:
                copy_transposed(t, [0])
                top_network(t - 1)
                copy_transposed(t, range(1, BLOCKS))
            top_network(TILES - 1)

        @block.vector
        def _(dve):
            def refill_indices(t, b):
                nc.vector.tensor_copy(tile_idx[:, b * BG:(b + 1) * BG],
                                      row_idx[:, bass.ds(t * SLOTS + b * BG, BG)]).then_inc(idx_ready, 1)

            def extract_tile(t, feat_used, more):
                if feat_used:
                    dve.wait_ge(l1_done, t)
                nc.vector.tensor_copy(feat[0:DENSE, 0, :], dense_sb[:, bass.ds(t * TILE, TILE)])
                for b in range(BLOCKS):
                    dve.wait_ge(dots_done, t * BLOCKS + b + 1)
                    if more:
                        refill_indices(t + 1, b)
                    for e in range(EX):
                        for q in range(EX):
                            first = 1 if q == 0 else 0
                            src = dots_ps[b % 2][e * F:(e + 1) * F, :, e * F + q * QJ + first:e * F + (q + 1) * QJ]
                            dst = feat[q * F:(q + 1) * F, first:QJ, b * BE:(b + 1) * BE]
                            dst = dst.rearrange("i j (g e) -> i g j e", e=EX)[:, :, :, e]
                            last = nc.vector.tensor_copy(dst, src)
                    last.then_inc(extracted, 1)

            nc.vector.memset(feat[0:F, 0, :], 0.0).then_inc(feat_cleared, 1)
            dve.wait_ge(ids_loaded, 32)
            nc.vector.tensor_tensor(row_idx[:], ids_sb[:], base_sb[:], ALU.add).then_inc(idx_based, 1)
            dve.wait_ge(idx_based, 1)
            for b in range(BLOCKS):
                refill_indices(0, b)
            dve.wait_ge(dense_loaded, 16)
            dve.wait_ge(feat_cleared, 1)
            extract_tile(0, False, True)
            with dve.Fori(1, TILES - 1) as t:
                extract_tile(t, True, True)
            extract_tile(TILES - 1, True, False)


def kernel(**inputs):
    import numpy as np
    import concourse.bacc as bacc
    from concourse.bass_utils import run_bass_kernel_spmd

    tables = [np.asarray(inputs[f"tbl_{f}"]) for f in range(F)]
    base = np.cumsum([0] + [t.shape[0] for t in tables[:-1]]).astype(np.int32)

    w_top1 = np.asarray(inputs["W_top1"])
    pairs = F * (F - 1) // 2
    lower, upper = np.triu_indices(F, k=1)
    w1 = np.zeros((EX, F, QJ, H1), w_top1.dtype)
    w1[upper // QJ, lower, upper % QJ] = w_top1[:pairs]
    w1[0, :DENSE, 0] = w_top1[pairs:]

    def chunks(w, n):
        return np.ascontiguousarray(np.asarray(w).reshape(n, P, -1).transpose(1, 0, 2))

    arrays = {
        "tables": np.concatenate(tables, axis=0),
        "row_ids": np.ascontiguousarray(np.asarray(inputs["ids"]).reshape(B // EX, P).T),
        "row_base": np.ascontiguousarray(np.broadcast_to(np.tile(base, EX)[:, None], (P, B // EX))),
        "dense_t": np.ascontiguousarray(np.asarray(inputs["dense_ctx"]).T),
        "identity": np.eye(P, dtype=np.float32),
        "w1": w1.reshape(P, QJ, H1),
        "b1": chunks(inputs["b_top1"], N1)[:, :, 0],
        "w2": chunks(inputs["W_top2"], N1),
        "b2": chunks(inputs["b_top2"], N2)[:, :, 0],
        "w3": chunks(inputs["W_top3"], N2)[:, :, 0],
    }
    arrays = {name: np.ascontiguousarray(a) for name, a in arrays.items()}
    nc = bacc.Bacc("TRN2", target_bir_lowering=False, num_devices=1)
    aps = {name: nc.dram_tensor(name, a.shape, mybir.dt.from_np(a.dtype), kind="ExternalInput").ap()
           for name, a in arrays.items()}
    y = nc.dram_tensor("y", (1, B), mybir.dt.float32, kind="ExternalOutput").ap()
    dlrm_program(nc, y=y, **aps)
    result = run_bass_kernel_spmd(nc, [arrays], core_ids=[0])
    return result.results[0]["y"].reshape(B, 1)
```

```python
from contextlib import ExitStack

import concourse.bass as bass
from concourse import mybir

P = 128
F = 32
D = 256
B = 512
DENSE = 16
H1, H2 = 512, 256
KD = D // P
EX = P // F
TILE = 128
TILES = B // TILE
SLOTS = TILE // EX
PAIRS = SLOTS // 2
BLOCKS = 4
BP = PAIRS // BLOCKS
BG = SLOTS // BLOCKS
BE = TILE // BLOCKS
QJ = F // EX
N1, N2 = H1 // P, H2 // P
L2_STEP, L3_STEP = 8, 11


def dlrm_program(nc, tables, row_ids, row_base, dense_t, identity, w1, b1, w2, b2, w3, y):
    f32, i32 = mybir.dt.float32, mybir.dt.int32
    ACT = mybir.ActivationFunctionType
    ALU = mybir.AluOpType

    with ExitStack() as ctx:
        def sb(name, shape, dt=f32):
            return ctx.enter_context(nc.sbuf_tensor(name, shape, dt))

        def ps(name, shape):
            return ctx.enter_context(nc.psum_tensor(name, shape, f32))

        def sem(name):
            return ctx.enter_context(nc.semaphore(name))

        ids_sb = sb("ids_sb", [P, B // EX], i32)
        base_sb = sb("base_sb", [P, B // EX], i32)
        row_idx = sb("row_idx", [P, B // EX], i32)
        tile_idx = sb("tile_idx", [P, SLOTS], i32)
        ident = sb("ident", [P, P])
        emb = sb("emb", [P, SLOTS, D])
        emb_t = sb("emb_t", [P, 2, 2, KD, P])
        feat = sb("feat", [P, QJ, TILE])
        dense_sb = sb("dense_sb", [DENSE, B])
        w1_sb = sb("w1_sb", [P, QJ, H1])
        w2_sb = sb("w2_sb", [P, N1, H2])
        w3_sb = sb("w3_sb", [P, N2])
        b1_sb = sb("b1_sb", [P, N1])
        b2_sb = sb("b2_sb", [P, N2])
        h1 = sb("h1", [P, N1, TILE])
        h2 = sb("h2", [P, N2, TILE])
        y_sb = sb("y_sb", [1, B])

        tr_ps = [ps(f"tr_ps{i}", [P, 2, KD, P]) for i in range(2)]
        dots_ps = [ps(f"dots_ps{i}", [P, BG, P]) for i in range(2)]
        top_ps = [ps(f"top_ps{i}", [P, 4, P]) for i in range(2)]

        ids_loaded = sem("ids_loaded")
        ident_loaded = sem("ident_loaded")
        dense_loaded = sem("dense_loaded")
        weights_loaded = sem("weights_loaded")
        idx_based = sem("idx_based")
        idx_ready = sem("idx_ready")
        gathered = [sem(f"gathered{p}") for p in range(PAIRS)]
        blocks_begun = sem("blocks_begun")
        transposed = sem("transposed")
        emb_t_ready = sem("emb_t_ready")
        dots_done = sem("dots_done")
        extracted_act = sem("extracted_act")
        extracted_dve = sem("extracted_dve")
        feat_cleared = sem("feat_cleared")
        l1_done = sem("l1_done")
        h1_ready = sem("h1_ready")
        l2_done = sem("l2_done")
        h2_ready = sem("h2_ready")
        l3_done = sem("l3_done")
        y_ready = sem("y_ready")
        y_stored = sem("y_stored")

        block = ctx.enter_context(nc.Block())

        @block.sync
        def _(sp):
            sp.dma_start(ids_sb[:], row_ids).then_inc(ids_loaded, 16)
            sp.dma_start(base_sb[:], row_base).then_inc(ids_loaded, 16)
            sp.dma_start(ident[:], identity).then_inc(ident_loaded, 16)
            sp.dma_start(dense_sb[:], dense_t).then_inc(dense_loaded, 16)
            sp.wait_ge(transposed, 1)
            sp.dma_start(w1_sb[:], w1).then_inc(weights_loaded, 16)
            sp.dma_start(w2_sb[:], w2).then_inc(weights_loaded, 16)
            sp.dma_start(w3_sb[:], w3).then_inc(weights_loaded, 16)
            sp.dma_start(b1_sb[:], b1).then_inc(weights_loaded, 16)
            sp.dma_start(b2_sb[:], b2).then_inc(weights_loaded, 16)
            sp.wait_ge(y_ready, TILES)
            sp.dma_start(y, y_sb[:]).then_inc(y_stored, 16)
            sp.wait_ge(y_stored, 16)

        @block.gpsimd
        def _(pool):
            def gather_tile(t, ring_used):
                for slot in range(SLOTS):
                    if slot % BG == 0:
                        b = slot // BG
                        pool.wait_ge(idx_ready, t * BLOCKS + b + 1)
                        if ring_used:
                            pool.wait_ge(transposed, (t - 1) * PAIRS + (b + 1) * BP)
                        pool.sem_inc(blocks_begun, 1)
                    nc.gpsimd.indirect_dma_start(
                        emb[:, slot, :], None, tables,
                        bass.IndirectOffsetOnAxis(tile_idx[:, slot:slot + 1], 0),
                    ).then_inc(gathered[slot // 2], 16)

            gather_tile(0, False)
            with pool.Fori(1, TILES) as t:
                gather_tile(t, True)

        @block.tensor
        def _(pe):
            def transpose_pair(t, p):
                pe.wait_ge(gathered[p], 32 * t + 32)
                for s in range(2):
                    for c in range(KD):
                        last = nc.tensor.transpose(tr_ps[p % 2][:, s, c, :],
                                                   emb[:, 2 * p + s, c * P:(c + 1) * P], ident[:])
                last.then_inc(transposed, 1)

            def dots_of_pair(t, p, buffer_used=True):
                b = p // BP
                pe.wait_ge(emb_t_ready, t * PAIRS + p + 1)
                if p % BP == 0 and buffer_used:
                    pe.wait_ge(extracted_act, t * BLOCKS + b - 1)
                    pe.wait_ge(extracted_dve, t * BLOCKS + b - 1)
                for s in range(2):
                    for c in range(KD):
                        operand = emb_t[:, p % 2, s, c, :]
                        last = nc.tensor.matmul(dots_ps[b % 2][:, 2 * (p % BP) + s, :], operand, operand,
                                                start=(c == 0), stop=(c == KD - 1))
                if p % BP == BP - 1:
                    last.then_inc(dots_done, 1)

            def layer1(t, n, relu_before):
                if n == 0:
                    pe.wait_ge(extracted_act, (t + 1) * BLOCKS)
                    pe.wait_ge(extracted_dve, (t + 1) * BLOCKS)
                if relu_before:
                    pe.wait_ge(h1_ready, t * N1 + n - 1)
                for j in range(QJ):
                    last = nc.tensor.matmul(top_ps[n % 2][:, n // 2, 0:TILE], w1_sb[:, j, n * P:(n + 1) * P],
                                            feat[:, j, :], start=(j == 0), stop=(j == QJ - 1))
                last.then_inc(l1_done, 1)

            def layer2(t):
                pe.wait_ge(h1_ready, (t + 1) * N1)
                for n in range(N2):
                    for k in range(N1):
                        last = nc.tensor.matmul(top_ps[n % 2][:, 2, 0:TILE], w2_sb[:, k, n * P:(n + 1) * P],
                                                h1[:, k, :], start=(k == 0), stop=(k == N1 - 1))
                    last.then_inc(l2_done, 1)

            def layer3(t):
                pe.wait_ge(h2_ready, (t + 1) * N2)
                for k in range(N2):
                    last = nc.tensor.matmul(top_ps[0][0:1, 3, 0:TILE], w3_sb[:, k:k + 1], h2[:, k, :],
                                            start=(k == 0), stop=(k == N2 - 1))
                last.then_inc(l3_done, 1)

            def tile(t, first):
                for p in range(PAIRS):
                    transpose_pair(t, p)
                    if p > 0:
                        dots_of_pair(t, p - 1, not first or p > 2 * BP)
                    elif not first:
                        dots_of_pair(t - 1, PAIRS - 1)
                    if not first:
                        if 1 <= p <= N1:
                            layer1(t - 1, p - 1, p > 2)
                        if p == L2_STEP:
                            layer2(t - 1)
                        if p == L3_STEP:
                            layer3(t - 1)

            pe.wait_ge(ident_loaded, 16)
            tile(0, True)
            pe.wait_ge(weights_loaded, 5 * 16)
            with pe.Fori(1, TILES) as t:
                tile(t, False)
            dots_of_pair(TILES - 1, PAIRS - 1)
            for n in range(N1):
                layer1(TILES - 1, n, n >= 2)
            layer2(TILES - 1)
            layer3(TILES - 1)

        def blocks_out(b, e):
            for q in range(EX):
                first = 1 if q == 0 else 0
                src = dots_ps[b % 2][e * F:(e + 1) * F, :, e * F + q * QJ + first:e * F + (q + 1) * QJ]
                dst = feat[q * F:(q + 1) * F, first:QJ, b * BE:(b + 1) * BE]
                yield dst.rearrange("i j (g e) -> i g j e", e=EX)[:, :, :, e], src

        @block.scalar
        def _(act):
            def copy_transposed(t, p):
                act.wait_ge(transposed, t * PAIRS + p + 1)
                nc.scalar.copy(emb_t[:, p % 2, :, :, :], tr_ps[p % 2][:, :, :, :]).then_inc(emb_t_ready, 1)

            def extract(t, b, feat_used):
                act.wait_ge(dots_done, t * BLOCKS + b + 1)
                if feat_used:
                    act.wait_ge(l1_done, t * N1)
                for e in range(EX // 2, EX):
                    for dst, src in blocks_out(b, e):
                        last = nc.scalar.copy(dst, src)
                last.then_inc(extracted_act, 1)

            def relu1(t, n):
                act.wait_ge(l1_done, t * N1 + n + 1)
                nc.scalar.activation(h1[:, n, :], top_ps[n % 2][:, n // 2, 0:TILE], ACT.Relu,
                                     bias=b1_sb[:, n:n + 1]).then_inc(h1_ready, 1)

            def relu2(t):
                for n in range(N2):
                    act.wait_ge(l2_done, t * N2 + n + 1)
                    nc.scalar.activation(h2[:, n, :], top_ps[n % 2][:, 2, 0:TILE], ACT.Relu,
                                         bias=b2_sb[:, n:n + 1]).then_inc(h2_ready, 1)

            def copy_y(t):
                act.wait_ge(l3_done, t + 1)
                nc.scalar.copy(y_sb[:, bass.ds(t * TILE, TILE)], top_ps[0][0:1, 3, 0:TILE]).then_inc(y_ready, 1)

            def tile(t, first):
                for p in range(PAIRS):
                    copy_transposed(t, p)
                    if p == 1 and not first:
                        extract(t - 1, BLOCKS - 1, False)
                    if p > 1 and p % BP == 1:
                        b = p // BP - 1
                        extract(t, b, b == 0 and not first)
                    if not first:
                        if 1 <= p <= N1:
                            relu1(t - 1, p - 1)
                        if p == L2_STEP + 1:
                            relu2(t - 1)
                        if p == L3_STEP + 1:
                            copy_y(t - 1)

            tile(0, True)
            act.wait_ge(weights_loaded, 5 * 16)
            with act.Fori(1, TILES) as t:
                tile(t, False)
            extract(TILES - 1, BLOCKS - 1, False)
            for n in range(N1):
                relu1(TILES - 1, n)
            relu2(TILES - 1)
            copy_y(TILES - 1)

        @block.vector
        def _(dve):
            def refill_indices(t, b):
                nc.vector.tensor_copy(tile_idx[:, b * BG:(b + 1) * BG],
                                      row_idx[:, bass.ds(t * SLOTS + b * BG, BG)]).then_inc(idx_ready, 1)

            def extract(t, b, feat_used, refill_tile):
                dve.wait_ge(dots_done, t * BLOCKS + b + 1)
                if refill_tile is not None:
                    refill_indices(refill_tile, b)
                if feat_used:
                    dve.wait_ge(l1_done, t * N1)
                if b == 0:
                    nc.vector.tensor_copy(feat[0:DENSE, 0, :], dense_sb[:, bass.ds(t * TILE, TILE)])
                for e in range(EX // 2):
                    for dst, src in blocks_out(b, e):
                        last = nc.vector.tensor_copy(dst, src)
                last.then_inc(extracted_dve, 1)

            nc.vector.memset(feat[0:F, 0, :], 0.0).then_inc(feat_cleared, 1)
            dve.wait_ge(ids_loaded, 32)
            nc.vector.tensor_tensor(row_idx[:], ids_sb[:], base_sb[:], ALU.add).then_inc(idx_based, 1)
            dve.wait_ge(idx_based, 1)
            for b in range(BLOCKS):
                refill_indices(0, b)
            dve.wait_ge(dense_loaded, 16)
            dve.wait_ge(feat_cleared, 1)
            for b in range(BLOCKS - 1):
                extract(0, b, False, 1)
            with dve.Fori(1, TILES - 1) as t:
                extract(t - 1, BLOCKS - 1, False, t)
                for b in range(BLOCKS - 1):
                    extract(t, b, b == 0, t + 1)
            extract(TILES - 2, BLOCKS - 1, False, TILES - 1)
            for b in range(BLOCKS):
                extract(TILES - 1, b, b == 0, None)


def kernel(**inputs):
    import numpy as np
    import concourse.bacc as bacc
    from concourse.bass_utils import run_bass_kernel_spmd

    tables = [np.asarray(inputs[f"tbl_{f}"]) for f in range(F)]
    base = np.cumsum([0] + [t.shape[0] for t in tables[:-1]]).astype(np.int32)

    w_top1 = np.asarray(inputs["W_top1"])
    pairs = F * (F - 1) // 2
    lower, upper = np.triu_indices(F, k=1)
    w1 = np.zeros((EX, F, QJ, H1), w_top1.dtype)
    w1[upper // QJ, lower, upper % QJ] = w_top1[:pairs]
    w1[0, :DENSE, 0] = w_top1[pairs:]

    def chunks(w, n):
        return np.ascontiguousarray(np.asarray(w).reshape(n, P, -1).transpose(1, 0, 2))

    arrays = {
        "tables": np.concatenate(tables, axis=0),
        "row_ids": np.ascontiguousarray(np.asarray(inputs["ids"]).reshape(B // EX, P).T),
        "row_base": np.ascontiguousarray(np.broadcast_to(np.tile(base, EX)[:, None], (P, B // EX))),
        "dense_t": np.ascontiguousarray(np.asarray(inputs["dense_ctx"]).T),
        "identity": np.eye(P, dtype=np.float32),
        "w1": w1.reshape(P, QJ, H1),
        "b1": chunks(inputs["b_top1"], N1)[:, :, 0],
        "w2": chunks(inputs["W_top2"], N1),
        "b2": chunks(inputs["b_top2"], N2)[:, :, 0],
        "w3": chunks(inputs["W_top3"], N2)[:, :, 0],
    }
    arrays = {name: np.ascontiguousarray(a) for name, a in arrays.items()}
    nc = bacc.Bacc("TRN2", target_bir_lowering=False, num_devices=1)
    aps = {name: nc.dram_tensor(name, a.shape, mybir.dt.from_np(a.dtype), kind="ExternalInput").ap()
           for name, a in arrays.items()}
    y = nc.dram_tensor("y", (1, B), mybir.dt.float32, kind="ExternalOutput").ap()
    dlrm_program(nc, y=y, **aps)
    result = run_bass_kernel_spmd(nc, [arrays], core_ids=[0])
    return result.results[0]["y"].reshape(B, 1)
```

```python
from contextlib import ExitStack

import concourse.bass as bass
from concourse import mybir

P = 128
F = 32
D = 256
B = 512
DENSE = 16
H1, H2 = 512, 256
KD = D // P

FH = 4
HOT_ROWS = 1000
HP, HC = 125, 8
HH = HC // 2

UNIT = 32
FS = P // UNIT
SLOTS = F // FS
PAIRS = SLOTS // 2
TILE = 128
TILES = B // TILE
UNITS = TILE // UNIT
HOT_UNIT = UNITS - 1
HOT_B = B - HOT_UNIT * UNIT
EX = P // F
GROUPS = UNIT // EX
QJ = F // EX
N1, N2 = H1 // P, H2 // P
HI, LO = 0, 1


def dlrm_program(nc, tables, row_ids, row_base, hot_ids, hot_row_number, dense_t, identity,
                 w1, w1_dense, b1, w2, b2, w3, y):
    f32, f32r, i32 = mybir.dt.float32, mybir.dt.float32r, mybir.dt.int32
    ACT = mybir.ActivationFunctionType
    ALU = mybir.AluOpType

    with ExitStack() as ctx:
        def sb(name, shape, dt=f32):
            return ctx.enter_context(nc.sbuf_tensor(name, shape, dt))

        def ps(name, shape):
            return ctx.enter_context(nc.psum_tensor(name, shape, f32))

        def sem(name):
            return ctx.enter_context(nc.semaphore(name))

        ids_sb = sb("ids_sb", [P, TILES * UNITS * SLOTS], i32)
        base_sb = sb("base_sb", [P, TILES * UNITS * SLOTS], i32)
        row_idx = sb("row_idx", [P, TILES * UNITS * SLOTS], i32)
        hot_ids_sb = sb("hot_ids_sb", [HP, FH, HOT_B], i32)
        hot_row_sb = sb("hot_row_sb", [HP, HC])
        one_hot = sb("one_hot", [HP, 3, HC, HOT_B], f32r)
        hot_table = sb("hot_table", [HP, 2, 2, HC, D], f32r)
        hot_t = sb("hot_t", [P, KD, HOT_B, FH])
        ident = sb("ident", [P, P])
        emb = sb("emb", [P, UNITS * SLOTS, D])
        emb_t = sb("emb_t", [P, 2, 2, KD, UNIT, F], f32r)
        feat = sb("feat", [P, QJ, B])
        dense_sb = sb("dense_sb", [DENSE, B])
        w1_sb = sb("w1_sb", [P, QJ, H1])
        w1_dense_sb = sb("w1_dense_sb", [DENSE, H1])
        w2_sb = sb("w2_sb", [P, N1, H2])
        w3_sb = sb("w3_sb", [P, N2])
        b1_sb = sb("b1_sb", [P, N1])
        b2_sb = sb("b2_sb", [P, N2])
        h1 = sb("h1", [P, N1, TILE])
        h2 = sb("h2", [P, N2, TILE])
        y_sb = sb("y_sb", [1, B])

        def staged(f, half):
            words = HH * D
            place = w1_sb[0:HP, :, :].rearrange("p a b -> p (a b)")
            return place[:, (f % 2 * 2 + half) * words:(f % 2 * 2 + half + 1) * words]

        def hot_part(f, half, part):
            return hot_table[:, f % 2, part, half * HH:(half + 1) * HH, :].rearrange("p k d -> p (k d)")

        tr_ps = [ps(f"tr_ps{i}", [P, KD, UNIT, 2 * FS]) for i in range(2)]
        dots_ps = ps("dots_ps", [P, GROUPS, 2, P])
        top_ps = [ps(f"top_ps{i}", [P, 4, TILE]) for i in range(2)]

        def hot_ps(c):
            return top_ps[c][:].rearrange("p a b -> p (a b)")[:, 0:HOT_B]

        ids_loaded = sem("ids_loaded")
        hot_row_loaded = sem("hot_row_loaded")
        hot_ids_loaded = [sem(f"hot_ids_loaded{f}") for f in range(FH)]
        table_loaded = [[sem(f"table_loaded{f}_{half}") for half in range(2)] for f in range(FH)]
        ident_loaded = sem("ident_loaded")
        biases_loaded = sem("biases_loaded")
        weights_loaded = sem("weights_loaded")
        idx_based = sem("idx_based")
        gathered = [[sem(f"gathered{u}_{p}") for p in range(PAIRS)] for u in range(UNITS)]
        one_hot_ready = sem("one_hot_ready")
        hi_split = sem("hi_split")
        lo_split = sem("lo_split")
        hot_done = sem("hot_done")
        hot_copied = sem("hot_copied")
        transposed = sem("transposed")
        pair_hi = sem("pair_hi")
        pair_lo = sem("pair_lo")
        hot_hi = sem("hot_hi")
        hot_lo = sem("hot_lo")
        dots_done = sem("dots_done")
        hi_lo_out = sem("hi_lo_out")
        extracted = sem("extracted")
        l1_done = sem("l1_done")
        h1_ready = sem("h1_ready")
        l2_done = sem("l2_done")
        h2_ready = sem("h2_ready")
        l3_done = sem("l3_done")
        y_ready = sem("y_ready")
        y_stored = sem("y_stored")

        WEIGHT_LOADS = 4 + QJ

        MIDDLE_UNITS = [(t, u) for t in range(1, TILES) for u in range(UNITS)][:-1]

        def all_gathered(t, u):
            return t * UNITS + u < HOT_UNIT

        def layer1_chunks(t, u):
            if t == TILES - 1:
                return ([], [0, 1], [2], [3])[u]
            return ([], [0], [1, 2], [3])[u]

        block = ctx.enter_context(nc.Block())

        @block.sync
        def _(sp):
            sp.dma_start(ids_sb[:], row_ids).then_inc(ids_loaded, 16)
            sp.dma_start(hot_row_sb[:], hot_row_number).then_inc(hot_row_loaded, 16)
            for f in range(2):
                sp.dma_start(hot_ids_sb[:, f, :], hot_ids[f].partition_broadcast(HP)).then_inc(hot_ids_loaded[f], 16)
            for f in range(FH):
                if f >= 2:
                    sp.wait_ge(lo_split, 2 * (f - 1))
                first_row = tables.shape[0] - (FH - f) * HOT_ROWS
                table = tables[first_row:first_row + HOT_ROWS, :].rearrange("(p h k) d -> h p (k d)", h=2, k=HH)
                for half in range(2):
                    if f > 0:
                        sp.wait_ge(transposed, (f - 1) * PAIRS + half + 2)
                    sp.dma_start(staged(f, half), table[half]).then_inc(table_loaded[f][half], 16)
                if f == 0:
                    sp.dma_start(ident[:], identity).then_inc(ident_loaded, 16)
                    sp.wait_ge(transposed, 1)
                if f < 2:
                    sp.dma_start(hot_ids_sb[:, f + 2, :],
                                 hot_ids[f + 2].partition_broadcast(HP)).then_inc(hot_ids_loaded[f + 2], 16)
            sp.dma_start(dense_sb[:], dense_t).then_inc(weights_loaded, 16)
            sp.dma_start(w1_dense_sb[:], w1_dense).then_inc(weights_loaded, 16)
            sp.dma_start(w2_sb[:], w2).then_inc(weights_loaded, 16)
            sp.dma_start(w3_sb[:], w3).then_inc(weights_loaded, 16)
            sp.dma_start(b1_sb[:], b1).then_inc(biases_loaded, 16)
            sp.dma_start(b2_sb[:], b2).then_inc(biases_loaded, 16)
            sp.wait_ge(lo_split, 2 * FH)
            for j in range(QJ):
                sp.wait_ge(transposed, (UNITS - 1) * PAIRS + 1 + j // 2)
                sp.dma_start(w1_sb[:, j, :], w1[:, j, :]).then_inc(weights_loaded, 16)
            sp.wait_ge(y_ready, TILES)
            sp.dma_start(y, y_sb[:]).then_inc(y_stored, 16)
            sp.wait_ge(y_stored, 16)

        @block.gpsimd
        def _(pool):
            pool.wait_ge(idx_based, 1)
            for t in range(TILES):
                for u in range(UNITS):
                    if t > 0:
                        pool.wait_ge(transposed, ((t - 1) * UNITS + u + 1) * PAIRS)
                    for s in range(SLOTS if all_gathered(t, u) else SLOTS - 1):
                        column = (t * UNITS + u) * SLOTS + s
                        nc.gpsimd.indirect_dma_start(
                            emb[:, u * SLOTS + s, :], None, tables,
                            bass.IndirectOffsetOnAxis(row_idx[:, column:column + 1], 0),
                        ).then_inc(gathered[u][s // 2], 16)

        @block.tensor
        def _(pe):
            def select_hot(f, c):
                if f > 0:
                    pe.wait_ge(hot_copied, (f - 1) * KD + c + 1)
                for half in range(2):
                    if c == 0:
                        pe.wait_ge(one_hot_ready, 2 * f + half + 1)
                        pe.wait_ge(lo_split, 2 * f + half + 1)
                    for part in (HI, LO):
                        for k in range(half * HH, (half + 1) * HH):
                            last = nc.tensor.matmul(hot_ps(c), hot_table[:, f % 2, part, k, c * P:(c + 1) * P],
                                                    one_hot[:, f % 3, k, :], start=(part == HI and k == 0),
                                                    stop=(part == LO and k == HC - 1))
                last.then_inc(hot_done, 1)

            def transpose_pair(t, u, p):
                if p < PAIRS - 1:
                    pe.wait_ge(gathered[u][p], 32 * t + 32)
                else:
                    pe.wait_ge(gathered[u][p], 16 * t + (32 if all_gathered(0, u) else 16))
                if t > 0 or u > 0 or p > 1:
                    pe.wait_ge(pair_lo, (t * UNITS + u) * PAIRS + p - 1)
                slots = (2 * p, 2 * p + 1) if p < PAIRS - 1 or all_gathered(t, u) else (2 * p,)
                for s in slots:
                    for c in range(KD):
                        last = nc.tensor.transpose(tr_ps[p % 2][:, c, :, (s % 2) * FS:(s % 2 + 1) * FS],
                                                   emb[:, u * SLOTS + s, c * P:(c + 1) * P], ident[:])
                last.then_inc(transposed, 1)

            def products(n):
                pe.wait_ge(pair_lo, (n + 1) * PAIRS)
                if n >= HOT_UNIT:
                    pe.wait_ge(hot_lo, n - HOT_UNIT + 1)
                if n > 0:
                    pe.wait_ge(extracted, n)
                for g in range(GROUPS):
                    for c in range(KD):
                        group = emb_t[:, n % 2, :, c, g * EX:(g + 1) * EX, :].rearrange("p a e f -> p a (e f)")
                        last = nc.tensor.matmul(dots_ps[:, g, :, :], group[:, HI, :], group,
                                                start=(c == 0), stop=(c == KD - 1))
                last.then_inc(dots_done, 1)

            def start_layer1(t, m):
                if t == 0 and m == 0:
                    pe.wait_ge(weights_loaded, WEIGHT_LOADS * 16)
                if t > 0 and m == 0:
                    pe.wait_ge(y_ready, t)
                nc.tensor.matmul(top_ps[m % 2][:, m // 2, :], w1_dense_sb[:, m * P:(m + 1) * P],
                                 dense_sb[:, t * TILE:(t + 1) * TILE], start=True, stop=False)

            def layer1(t, m, started=False):
                out = top_ps[m % 2][:, m // 2, :]
                if m >= 2:
                    pe.wait_ge(h1_ready, t * N1 + m - 1)
                if not started:
                    start_layer1(t, m)
                if m == 0:
                    pe.wait_ge(extracted, (t + 1) * UNITS)
                for j in range(QJ):
                    last = nc.tensor.matmul(out, w1_sb[:, j, m * P:(m + 1) * P], feat[:, j, t * TILE:(t + 1) * TILE],
                                            start=False, stop=(j == QJ - 1))
                last.then_inc(l1_done, 1)

            def layer2(t, chunks=range(N2)):
                for m in chunks:
                    for k in range(N1):
                        if m == 0 and k % (N1 - 1) == 0:
                            pe.wait_ge(h1_ready, (t + 1) * N1 - (1 if k == 0 else 0))
                        last = nc.tensor.matmul(top_ps[m % 2][:, 2, :], w2_sb[:, k, m * P:(m + 1) * P],
                                                h1[:, k, :], start=(k == 0), stop=(k == N1 - 1))
                    last.then_inc(l2_done, 1)

            def layer3(t):
                for k in range(N2):
                    pe.wait_ge(h2_ready, t * N2 + k + 1)
                    last = nc.tensor.matmul(top_ps[0][0:1, 3, :], w3_sb[:, k:k + 1], h2[:, k, :],
                                            start=(k == 0), stop=(k == N2 - 1))
                last.then_inc(l3_done, 1)

            def first_tile():
                assert FH == UNITS
                for u in range(UNITS):
                    transpose_pair(0, u, 0)
                    transpose_pair(0, u, 1)
                    if u > 0:
                        products(u - 1)
                    select_hot(u, 0)
                    transpose_pair(0, u, 2)
                    transpose_pair(0, u, 3)
                    select_hot(u, 1)

            def unit(t, u):
                transpose_pair(t, u, 0)
                transpose_pair(t, u, 1)
                if u == 1 and t > 1:
                    layer3(t - 2)
                products(t * UNITS + u - 1)
                transpose_pair(t, u, 2)
                transpose_pair(t, u, 3)
                if u == 0 and t > 1:
                    layer2(t - 2)
                for m in layer1_chunks(t, u):
                    layer1(t - 1, m)

            def last_unit():
                t, u = TILES - 1, UNITS - 1
                transpose_pair(t, u, 0)
                products(t * UNITS + u - 1)
                transpose_pair(t, u, 1)
                layer1(t - 1, N1 - 1)
                transpose_pair(t, u, 2)
                transpose_pair(t, u, 3)
                layer2(t - 1, [0])

            pe.wait_ge(ident_loaded, 16)
            first_tile()
            for t, u in MIDDLE_UNITS:
                unit(t, u)
            last_unit()
            products(TILES * UNITS - 1)
            layer2(TILES - 2, [1])
            layer3(TILES - 2)
            for m in (1, 0):
                start_layer1(TILES - 1, m)
            for m in range(N1):
                layer1(TILES - 1, m, m < 2)
            layer2(TILES - 1)
            layer3(TILES - 1)

        def blocks_out(part, t, u, e):
            for q in range(EX):
                src = dots_ps[e * F:(e + 1) * F, :, part, e * F + q * QJ:e * F + (q + 1) * QJ]
                dst = feat[q * F:(q + 1) * F, :, t * TILE + u * UNIT:t * TILE + (u + 1) * UNIT]
                yield dst.rearrange("i j (g e) -> i g j e", e=EX)[:, :, :, e], src

        def pair_copies(part, t, u, p):
            n = 2 * FS if p < PAIRS - 1 or all_gathered(t, u) else FS
            dst = emb_t[:, u % 2, part, :, :, 2 * p * FS:2 * p * FS + n]
            return dst.rearrange("p c e f -> p (c e) f"), tr_ps[p % 2][:, :, :, 0:n].rearrange("p c e f -> p (c e) f")

        def hot_view(part, u):
            return emb_t[:, u % 2, part, :, :, F - FH:F]

        def hot_unit(t, u):
            unit = t * UNITS + u - HOT_UNIT
            return hot_t[:, :, unit * UNIT:(unit + 1) * UNIT, :]

        @block.scalar
        def _(act):
            act.dma_start(base_sb[:], row_base).then_inc(ids_loaded, 16)

            def split_table(f):
                for half in range(2):
                    act.wait_ge(table_loaded[f][half], 16)
                    if f >= 2 and half == 0:
                        act.wait_ge(hot_done, (f - 1) * KD)
                    nc.scalar.copy(hot_part(f, half, HI), staged(f, half)).then_inc(hi_split, 1)

            def copy_hot(f, c):
                act.wait_ge(hot_done, f * KD + c + 1)
                nc.scalar.copy(hot_t[:, c, :, f], hot_ps(c)).then_inc(hot_copied, 1)

            def hi_pair(t, u, p):
                act.wait_ge(transposed, (t * UNITS + u) * PAIRS + p + 1)
                dst, src = pair_copies(HI, t, u, p)
                nc.scalar.copy(dst, src).then_inc(pair_hi, 1)

            def hi_hot(t, u):
                nc.scalar.copy(hot_view(HI, u), hot_unit(t, u)).then_inc(hot_hi, 1)

            def extract(t, u, examples=range(EX)):
                act.wait_ge(dots_done, t * UNITS + u + 1)
                for e in examples:
                    for dst, src in blocks_out(LO, t, u, e):
                        last = nc.scalar.copy(dst, src)
                    last.then_inc(hi_lo_out, 1)

            def extract_before(t, u, examples):
                extract(t if u > 0 else t - 1, (u - 1) % UNITS, examples)

            def relu1(t, m):
                act.wait_ge(l1_done, t * N1 + m + 1)
                nc.scalar.activation(h1[:, m, :], top_ps[m % 2][:, m // 2, :], ACT.Relu,
                                     bias=b1_sb[:, m:m + 1]).then_inc(h1_ready, 1)

            def relu2(t, chunks=range(N2)):
                for m in chunks:
                    act.wait_ge(l2_done, t * N2 + m + 1)
                    nc.scalar.activation(h2[:, m, :], top_ps[m % 2][:, 2, :], ACT.Relu,
                                         bias=b2_sb[:, m:m + 1]).then_inc(h2_ready, 1)

            def copy_y(t):
                act.wait_ge(l3_done, t + 1)
                nc.scalar.copy(y_sb[:, t * TILE:(t + 1) * TILE], top_ps[0][0:1, 3, :]).then_inc(y_ready, 1)

            def first_tile():
                for u in range(UNITS):
                    hi_pair(0, u, 0)
                    if u == 0:
                        split_table(0)
                    hi_pair(0, u, 1)
                    if u > 0:
                        extract(0, u - 1)
                    copy_hot(u, 0)
                    hi_pair(0, u, 2)
                    hi_pair(0, u, 3)
                    if u < FH - 1:
                        split_table(u + 1)
                    copy_hot(u, 1)
                act.wait_ge(hot_copied, FH * KD)
                hi_hot(0, UNITS - 1)

            def unit(t, u):
                hi_pair(t, u, 0)
                hi_pair(t, u, 1)
                hi_hot(t, u)
                if u == 1 and t > 1:
                    copy_y(t - 2)
                extract_before(t, u, [0, 1])
                hi_pair(t, u, 2)
                hi_pair(t, u, 3)
                extract_before(t, u, [2, 3])
                if u == 0 and t > 1:
                    relu2(t - 2)
                for m in layer1_chunks(t, u):
                    relu1(t - 1, m)

            def last_unit():
                t, u = TILES - 1, UNITS - 1
                hi_pair(t, u, 0)
                hi_hot(t, u)
                extract(t, u - 1, [0, 1])
                hi_pair(t, u, 1)
                extract(t, u - 1, [2, 3])
                relu1(t - 1, N1 - 1)
                hi_pair(t, u, 2)
                hi_pair(t, u, 3)
                relu2(t - 1, [0])

            first_tile()
            act.wait_ge(biases_loaded, 32)
            for t, u in MIDDLE_UNITS:
                unit(t, u)
            last_unit()
            extract(TILES - 1, UNITS - 1, [0, 1])
            relu2(TILES - 2, [1])
            extract(TILES - 1, UNITS - 1, [2, 3])
            copy_y(TILES - 2)
            for m in range(N1):
                relu1(TILES - 1, m)
            relu2(TILES - 1)
            copy_y(TILES - 1)

        @block.vector
        def _(dve):
            def build_one_hot(f, half):
                if half == 0:
                    dve.wait_ge(hot_ids_loaded[f], 16)
                    if f >= 3:
                        dve.wait_ge(hot_done, (f - 2) * KD)
                for k in range(half * HH, (half + 1) * HH):
                    last = nc.vector.tensor_scalar(one_hot[:, f % 3, k, :], hot_ids_sb[:, f, :],
                                                   hot_row_sb[:, k:k + 1], None, ALU.is_equal)
                last.then_inc(one_hot_ready, 1)

            def split_table(f):
                for half in range(2):
                    dve.wait_ge(hi_split, 2 * f + half + 1)
                    nc.vector.tensor_tensor(hot_part(f, half, LO), staged(f, half),
                                            hot_part(f, half, HI).bitcast(f32), ALU.subtract).then_inc(lo_split, 1)

            def lo_pair(t, u, p):
                dve.wait_ge(pair_hi, (t * UNITS + u) * PAIRS + p + 1)
                dst, src = pair_copies(LO, t, u, p)
                hi, _ = pair_copies(HI, t, u, p)
                nc.vector.tensor_tensor(dst, src, hi.bitcast(f32), ALU.subtract).then_inc(pair_lo, 1)

            def lo_hot(t, u):
                dve.wait_ge(hot_hi, t * UNITS + u - HOT_UNIT + 1)
                nc.vector.tensor_tensor(hot_view(LO, u), hot_unit(t, u), hot_view(HI, u).bitcast(f32),
                                        ALU.subtract).then_inc(hot_lo, 1)

            def extract(t, u, examples=range(EX)):
                for e in examples:
                    dve.wait_ge(hi_lo_out, (t * UNITS + u) * EX + e + 1)
                    for dst, src in blocks_out(HI, t, u, e):
                        last = nc.vector.scalar_tensor_tensor(out=dst, in0=src, scalar=0.5, in1=dst,
                                                              op0=ALU.mult, op1=ALU.add)
                if EX - 1 in examples:
                    last.then_inc(extracted, 1)

            def extract_before(t, u, examples):
                extract(t if u > 0 else t - 1, (u - 1) % UNITS, examples)

            def unit(t, u):
                lo_pair(t, u, 0)
                lo_pair(t, u, 1)
                lo_hot(t, u)
                extract_before(t, u, [0, 1])
                lo_pair(t, u, 2)
                lo_pair(t, u, 3)
                extract_before(t, u, [2, 3])

            def last_unit():
                t, u = TILES - 1, UNITS - 1
                lo_pair(t, u, 0)
                lo_hot(t, u)
                extract(t, u - 1, [0, 1])
                lo_pair(t, u, 1)
                extract(t, u - 1, [2, 3])
                lo_pair(t, u, 2)
                lo_pair(t, u, 3)

            def first_tile():
                for u in range(UNITS):
                    lo_pair(0, u, 0)
                    if u == 0:
                        split_table(0)
                    lo_pair(0, u, 1)
                    if u == 0:
                        build_one_hot(2, 0)
                        build_one_hot(2, 1)
                    else:
                        extract(0, u - 1)
                    if u == 1:
                        build_one_hot(3, 0)
                    lo_pair(0, u, 2)
                    lo_pair(0, u, 3)
                    if u + 1 < FH:
                        split_table(u + 1)
                    if u == 1:
                        build_one_hot(3, 1)
                lo_hot(0, UNITS - 1)

            dve.wait_ge(ids_loaded, 32)
            nc.vector.tensor_tensor(row_idx[:], ids_sb[:], base_sb[:], ALU.add).then_inc(idx_based, 1)
            dve.wait_ge(hot_row_loaded, 16)
            for f, half in ((0, 0), (0, 1), (1, 0), (1, 1)):
                build_one_hot(f, half)
            first_tile()
            for t, u in MIDDLE_UNITS:
                unit(t, u)
            last_unit()
            extract(TILES - 1, UNITS - 1)


def kernel(**inputs):
    import numpy as np
    import concourse.bacc as bacc
    from concourse.bass_utils import run_bass_kernel_spmd

    tables = [np.asarray(inputs[f"tbl_{f}"]) for f in range(F)]
    hot = [f for f in range(F) if tables[f].shape[0] == HOT_ROWS][:FH]
    order = [f for f in range(F) if f not in hot] + hot
    ids = np.asarray(inputs["ids"])

    row_ids = ids[:, order].reshape(TILES * UNITS, UNIT, SLOTS, FS).transpose(1, 3, 0, 2).reshape(P, -1)
    starts = np.cumsum([0] + [tables[f].shape[0] for f in order[:-1]]).astype(np.int32)
    row_base = np.broadcast_to(starts.reshape(SLOTS, FS).T[None, :, None, :], (UNIT, FS, TILES * UNITS, SLOTS))

    w_top1 = np.asarray(inputs["W_top1"])
    pairs = F * (F - 1) // 2
    slot = np.argsort(order)
    w1 = np.zeros((EX, F, QJ, H1), w_top1.dtype)
    for a, b in (np.triu_indices(F, k=1), np.triu_indices(F, k=1)[::-1]):
        w1[slot[b] // QJ, slot[a], slot[b] % QJ] = w_top1[:pairs]

    def chunks(w, n):
        return np.asarray(w).reshape(n, P, -1).transpose(1, 0, 2)

    arrays = {
        "tables": np.concatenate([tables[f] for f in order], axis=0),
        "row_ids": row_ids,
        "row_base": row_base.reshape(P, -1),
        "hot_ids": ids[HOT_UNIT * UNIT:, hot].T,
        "hot_row_number": np.arange(HOT_ROWS, dtype=np.float32).reshape(HP, HC),
        "dense_t": np.asarray(inputs["dense_ctx"]).T,
        "identity": np.eye(P, dtype=np.float32),
        "w1": w1.reshape(P, QJ, H1),
        "w1_dense": w_top1[pairs:],
        "b1": chunks(inputs["b_top1"], N1)[:, :, 0],
        "w2": chunks(inputs["W_top2"], N1),
        "b2": chunks(inputs["b_top2"], N2)[:, :, 0],
        "w3": chunks(inputs["W_top3"], N2)[:, :, 0],
    }
    arrays = {name: np.ascontiguousarray(a) for name, a in arrays.items()}
    nc = bacc.Bacc("TRN2", target_bir_lowering=False, num_devices=1)
    aps = {name: nc.dram_tensor(name, a.shape, mybir.dt.from_np(a.dtype), kind="ExternalInput").ap()
           for name, a in arrays.items()}
    y = nc.dram_tensor("y", (1, B), mybir.dt.float32, kind="ExternalOutput").ap()
    dlrm_program(nc, y=y, **aps)
    result = run_bass_kernel_spmd(nc, [arrays], core_ids=[0])
    return result.results[0]["y"].reshape(B, 1)
```
